# Optimizing a Trainium2 kernel written in Bass

```python
import numpy as np
import jax
import jax.numpy as jnp

def _softmax(x, axis=-1):
    return jax.nn.softmax(x, axis=axis)

def _gelu(x):
    return jax.nn.gelu(x, approximate=True)

def _silu(x):
    return jax.nn.silu(x)

def _sigmoid(x):
    return jax.nn.sigmoid(x)

def _layernorm(x, axis=-1, eps=1e-05):
    m = jnp.mean(x, axis=axis, keepdims=True)
    v = jnp.var(x, axis=axis, keepdims=True)
    return (x - m) / jnp.sqrt(v + eps)

def _scatter_add(tgt, idx, src, axis=0):
    return tgt.at[idx].add(src)

def _segment_sum(src, seg, n):
    return jax.ops.segment_sum(src, seg, n)
kernel_name = 'mk_dlrm_tower_d1_rec_r8_5b8383'

def setup_inputs(seed: int=0):
    np.random.seed(seed)
    _w = jnp.asarray

    def _rec_inputs():
        import jax
        import jax.numpy as jnp
        _tk = jax.random.key(seed)
        ids = jnp.stack([jax.random.randint(jax.random.fold_in(_tk, 200 + f), (2048,), 0, v, jnp.int32) for f, v in enumerate([125000, 1000, 1000, 12500, 12500, 12500, 12500, 1250, 12500, 12500, 1000, 12500, 1000, 1250, 12500, 1000, 12500, 1000, 1250, 1250, 1000, 1000, 1000, 1000, 1000, 1000])], axis=1)
        tbl_0 = 0.05 * jax.random.normal(jax.random.fold_in(_tk, 500 + 0), (125000, 128), jnp.float32)
        tbl_1 = 0.05 * jax.random.normal(jax.random.fold_in(_tk, 500 + 1), (1000, 128), jnp.float32)
        tbl_2 = 0.05 * jax.random.normal(jax.random.fold_in(_tk, 500 + 2), (1000, 128), jnp.float32)
        tbl_3 = 0.05 * jax.random.normal(jax.random.fold_in(_tk, 500 + 3), (12500, 128), jnp.float32)
        tbl_4 = 0.05 * jax.random.normal(jax.random.fold_in(_tk, 500 + 4), (12500, 128), jnp.float32)
        tbl_5 = 0.05 * jax.random.normal(jax.random.fold_in(_tk, 500 + 5), (12500, 128), jnp.float32)
        tbl_6 = 0.05 * jax.random.normal(jax.random.fold_in(_tk, 500 + 6), (12500, 128), jnp.float32)
        tbl_7 = 0.05 * jax.random.normal(jax.random.fold_in(_tk, 500 + 7), (1250, 128), jnp.float32)
        tbl_8 = 0.05 * jax.random.normal(jax.random.fold_in(_tk, 500 + 8), (12500, 128), jnp.float32)
        tbl_9 = 0.05 * jax.random.normal(jax.random.fold_in(_tk, 500 + 9), (12500, 128), jnp.float32)
        tbl_10 = 0.05 * jax.random.normal(jax.random.fold_in(_tk, 500 + 10), (1000, 128), jnp.float32)
        tbl_11 = 0.05 * jax.random.normal(jax.random.fold_in(_tk, 500 + 11), (12500, 128), jnp.float32)
        tbl_12 = 0.05 * jax.random.normal(jax.random.fold_in(_tk, 500 + 12), (1000, 128), jnp.float32)
        tbl_13 = 0.05 * jax.random.normal(jax.random.fold_in(_tk, 500 + 13), (1250, 128), jnp.float32)
        tbl_14 = 0.05 * jax.random.normal(jax.random.fold_in(_tk, 500 + 14), (12500, 128), jnp.float32)
        tbl_15 = 0.05 * jax.random.normal(jax.random.fold_in(_tk, 500 + 15), (1000, 128), jnp.float32)
        tbl_16 = 0.05 * jax.random.normal(jax.random.fold_in(_tk, 500 + 16), (12500, 128), jnp.float32)
        tbl_17 = 0.05 * jax.random.normal(jax.random.fold_in(_tk, 500 + 17), (1000, 128), jnp.float32)
        tbl_18 = 0.05 * jax.random.normal(jax.random.fold_in(_tk, 500 + 18), (1250, 128), jnp.float32)
        tbl_19 = 0.05 * jax.random.normal(jax.random.fold_in(_tk, 500 + 19), (1250, 128), jnp.float32)
        tbl_20 = 0.05 * jax.random.normal(jax.random.fold_in(_tk, 500 + 20), (1000, 128), jnp.float32)
        tbl_21 = 0.05 * jax.random.normal(jax.random.fold_in(_tk, 500 + 21), (1000, 128), jnp.float32)
        tbl_22 = 0.05 * jax.random.normal(jax.random.fold_in(_tk, 500 + 22), (1000, 128), jnp.float32)
        tbl_23 = 0.05 * jax.random.normal(jax.random.fold_in(_tk, 500 + 23), (1000, 128), jnp.float32)
        tbl_24 = 0.05 * jax.random.normal(jax.random.fold_in(_tk, 500 + 24), (1000, 128), jnp.float32)
        tbl_25 = 0.05 * jax.random.normal(jax.random.fold_in(_tk, 500 + 25), (1000, 128), jnp.float32)
        _rk = jax.random.fold_in(_tk, 7)
        r_dense_features = -0.000520686 + 1.00062 * jax.random.normal(jax.random.fold_in(_rk, 101), (2048, 128), jnp.float32)
        W_top1 = 0.0405887 * jax.random.normal(jax.random.fold_in(_tk, 801), (607, 512), jnp.float32)
        W_top2 = 0.0441942 * jax.random.normal(jax.random.fold_in(_tk, 802), (512, 256), jnp.float32)
        W_top3 = 0.0625 * jax.random.normal(jax.random.fold_in(_tk, 803), (256, 1), jnp.float32)
        b_top1 = jnp.zeros((512,), jnp.float32)
        b_top2 = jnp.zeros((256,), jnp.float32)
        return (r_dense_features, ids, tbl_0, tbl_1, tbl_2, tbl_3, tbl_4, tbl_5, tbl_6, tbl_7, tbl_8, tbl_9, tbl_10, tbl_11, tbl_12, tbl_13, tbl_14, tbl_15, tbl_16, tbl_17, tbl_18, tbl_19, tbl_20, tbl_21, tbl_22, tbl_23, tbl_24, tbl_25, W_top1, b_top1, W_top2, b_top2, W_top3)
    r_dense_features, ids, tbl_0, tbl_1, tbl_2, tbl_3, tbl_4, tbl_5, tbl_6, tbl_7, tbl_8, tbl_9, tbl_10, tbl_11, tbl_12, tbl_13, tbl_14, tbl_15, tbl_16, tbl_17, tbl_18, tbl_19, tbl_20, tbl_21, tbl_22, tbl_23, tbl_24, tbl_25, W_top1, b_top1, W_top2, b_top2, W_top3 = _rec_inputs()

    def _L0_rec_setup():
        import jax, jax.numpy as jnp
        import numpy as np
        B, F, D = (2048, 26, 128)
        key = jax.random.key(seed)
        k1, k2 = jax.random.split(key)
        dense_features = jax.random.normal(k1, (B, D), dtype=jnp.float32)
        sparse_values = jax.random.normal(k2, (B, F, D), dtype=jnp.float32)
        return {'dense_features': dense_features, 'sparse_values': sparse_values}
    _L0_rec_all = _L0_rec_setup()
    _L0_rec_in = {k: v for k, v in _L0_rec_all.items() if k in ()}
    del _L0_rec_all
    return {'r_dense_features': r_dense_features, 'ids': ids, 'tbl_0': tbl_0, 'tbl_1': tbl_1, 'tbl_2': tbl_2, 'tbl_3': tbl_3, 'tbl_4': tbl_4, 'tbl_5': tbl_5, 'tbl_6': tbl_6, 'tbl_7': tbl_7, 'tbl_8': tbl_8, 'tbl_9': tbl_9, 'tbl_10': tbl_10, 'tbl_11': tbl_11, 'tbl_12': tbl_12, 'tbl_13': tbl_13, 'tbl_14': tbl_14, 'tbl_15': tbl_15, 'tbl_16': tbl_16, 'tbl_17': tbl_17, 'tbl_18': tbl_18, 'tbl_19': tbl_19, 'tbl_20': tbl_20, 'tbl_21': tbl_21, 'tbl_22': tbl_22, 'tbl_23': tbl_23, 'tbl_24': tbl_24, 'tbl_25': tbl_25, 'W_top1': W_top1, 'b_top1': b_top1, 'W_top2': W_top2, 'b_top2': b_top2, 'W_top3': W_top3}

def reference(r_dense_features, ids, tbl_0, tbl_1, tbl_2, tbl_3, tbl_4, tbl_5, tbl_6, tbl_7, tbl_8, tbl_9, tbl_10, tbl_11, tbl_12, tbl_13, tbl_14, tbl_15, tbl_16, tbl_17, tbl_18, tbl_19, tbl_20, tbl_21, tbl_22, tbl_23, tbl_24, tbl_25, W_top1, b_top1, W_top2, b_top2, W_top3):
    import jax
    import jax.numpy as jnp

    def _L0_rec_ref(dense_features, sparse_values):
        import jax, jax.numpy as jnp
        import numpy as np
        B, F, D = (2048, 26, 128)
        sd = jnp.einsum('bfd,bd->bf', sparse_values, dense_features)
        ss = jnp.einsum('bfd,bgd->bfg', sparse_values, sparse_values)
        iu, ju = jnp.triu_indices(F, k=1)
        pairs = ss[:, iu, ju]
        return jnp.concatenate([dense_features, sd, pairs], axis=1)
    e = jnp.stack([tbl_0[ids[:, 0]], tbl_1[ids[:, 1]], tbl_2[ids[:, 2]], tbl_3[ids[:, 3]], tbl_4[ids[:, 4]], tbl_5[ids[:, 5]], tbl_6[ids[:, 6]], tbl_7[ids[:, 7]], tbl_8[ids[:, 8]], tbl_9[ids[:, 9]], tbl_10[ids[:, 10]], tbl_11[ids[:, 11]], tbl_12[ids[:, 12]], tbl_13[ids[:, 13]], tbl_14[ids[:, 14]], tbl_15[ids[:, 15]], tbl_16[ids[:, 16]], tbl_17[ids[:, 17]], tbl_18[ids[:, 18]], tbl_19[ids[:, 19]], tbl_20[ids[:, 20]], tbl_21[ids[:, 21]], tbl_22[ids[:, 22]], tbl_23[ids[:, 23]], tbl_24[ids[:, 24]], tbl_25[ids[:, 25]]], axis=1)
    z = _L0_rec_ref(r_dense_features, e)
    z = z.reshape(z.shape[0], -1)
    h = jnp.concatenate([z, r_dense_features], axis=1)
    h = jnp.maximum(h @ W_top1 + b_top1, 0.0)
    h = jnp.maximum(h @ W_top2 + b_top2, 0.0)
    y = h @ W_top3
    return y

_drawn_inputs = setup_inputs


def setup_inputs(seed=0):
    import zlib

    import numpy as np

    out = dict(_drawn_inputs(seed))
    spreads = {'b_top1': (0.0, 0.1), 'b_top2': (0.0, 0.1)}
    factors = {}
    for name, (base, spread) in spreads.items():
        noise = np.random.default_rng([zlib.crc32(name.encode()), seed]).standard_normal(out[name].shape)
        drawn = base * np.exp(spread * noise) if base else spread * noise
        out[name] = jnp.asarray(drawn.astype(out[name].dtype))
    for name, factor in factors.items():
        out[name] = (out[name] * factor).astype(out[name].dtype)
    return out
```

```python
from contextlib import ExitStack

import concourse.bass as bass
from concourse import mybir

B = 2048
F = 26
D = 128
P = 128
Q = 4
JJ = P // Q
NT = B // P
TS = 2
NS = NT // TS
SB = TS * P
SJ = TS * JJ
V = F + 1
GC = F
GB = 4
CH = 2 * GB
NC = JJ // CH
CS = TS * NC
HC = CS // 2
N1, N2 = 512, 256
NPAIR = F + F * (F - 1) // 2

LOOKED = (20, 21, 22, 23, 24, 25, 2)
VS = 1000
NK = 8
PK = VS // NK
NO = 4
HK = NK // NO
NX = len(LOOKED)
HS = NO * NX
GATHERED = [[(3, 7)], [(7, 11)], [(11, 15)], [(15, 19)], [(0, 2), (19, 20)]]
NB = len(GATHERED)
BATCH = [[f for run in runs for f in range(*run)] for runs in GATHERED]
SLOT = {f: n for n, f in enumerate(f for b in BATCH for f in b)}

ITEMS = ([("lookup", None, x) for x in range(0, NX, 2)]
         + [("rows", t, k) for t in range(TS) for k in range(NB)])
NP = (NX + 1) // 2
COPIER = ["act"] * NP + ["dve", "act"] * NB
BANK = [m % 3 for m in range(len(ITEMS))]
TILE_READY = [NP + NB, len(ITEMS)]

fp32 = mybir.dt.float32
fp32r = mybir.dt.float32r
int32 = mybir.dt.int32
ALU = mybir.AluOpType
ACT = mybir.ActivationFunctionType


def copied_by(engine, m):
    return COPIER[:m].count(engine)


NZ = 3
ZR = 126
BLOCKS = []
for _chunk, _firsts in enumerate(((0, 12, 24), (3, 15, 18), (6, 9, 21))):
    _row = 0
    for _c in _firsts:
        BLOCKS.append((_c, min(3, GC - _c), _chunk, _row))
        _row += (F - _c) * min(3, GC - _c)
    assert _row <= ZR


def pair_rows():
    start = [D]
    for c in range(GC):
        start.append(start[-1] + F - c)
    rows = [[None] * P for _ in range(NZ)]
    for first, width, chunk, row in BLOCKS:
        for v in range(first + 1, V):
            for c in range(first, first + width):
                if c < v:
                    rows[chunk][row + (v - first - 1) * width + c - first] = start[c] + v - c - 1
    return rows


def build(nc, dense, ids, ids_steps, tables, w1, b1, w2, b2, w3, out):
    ctx = ExitStack()
    with ctx:
        def sb(name, shape, dt=fp32):
            return ctx.enter_context(nc.sbuf_tensor(name, shape, dt))

        def pb(name, shape):
            return ctx.enter_context(nc.psum_tensor(name, shape, fp32))

        def sem(name):
            return ctx.enter_context(nc.semaphore(name))

        ids_all = sb("ids_all", [P, NT, F], int32)
        ids_cur = sb("ids_cur", [P, TS, F], int32)
        ids_row = sb("ids_row", [P, NX, SB], int32)
        block_no = ids_row[:].bitcast(fp32)
        minus_row = sb("minus_row", [P, 1], int32)
        minus_rowf = sb("minus_rowf", [P, 1])
        tab_hi = sb("tab_hi", [P, NX, NK, D], fp32r)
        tab_lo = sb("tab_lo", [P, NX, NK, D], fp32r)
        onehot = sb("onehot", [P, NO, HK, SB], fp32r)
        early = sb("early", [P, (1 + NZ) * N1])
        dense_all = early[:].rearrange("p (n d) -> p n d", n=NT)
        w1raw = early[:].rearrange("p (c n) -> p c n", n=N1)
        dense_t = sb("dense_t", [P, Q, NT * JJ])
        rows = sb("rows", [P, TS, len(SLOT), D])
        vec_t = sb("vec_t", [P, TS, JJ, Q, 32])
        gram = sb("gram", [P, GC, Q, SJ])
        z_hi = sb("z_hi", [P, 1 + NZ, SB], fp32r)
        z_lo = sb("z_lo", [P, 1 + NZ, SB], fp32r)
        z = z_lo[:].bitcast(fp32)
        w1_hi = sb("w1_hi", [P, 1 + NZ, N1], fp32r)
        w1_lo = sb("w1_lo", [P, 1 + NZ, N1], fp32r)
        w2s = sb("w2s", [P, N1 // P, N2])
        w3s = sb("w3s", [P, N2 // P])
        b1s = sb("b1s", [P, N1 // P])
        b2s = sb("b2s", [P, N2 // P])
        h1 = sb("h1", [P, N1 // P, SB])
        h2 = sb("h2", [P, N2 // P, SB])
        w1second = h2[:].rearrange("p c s -> p (c s)")
        y = sb("y", [P, 2, NS])
        y_t = sb("y_t", [2 * NS, P])
        ident = sb("ident", [P, P])
        NSTAGE = GC * SB // (NK * D)
        staged = gram[:].rearrange("p c q j -> p (c q j)")[:, 0:NSTAGE * NK * D].rearrange(
            "p (n e) -> p n e", n=NSTAGE)

        ps_t = [pb(f"ps_t{i}", [P, 4, P]) for i in range(3)]
        ps_g = [pb(f"ps_g{i}", [P, 2, 512]) for i in range(2)]
        ps_h = pb("ps_h", [P, 2, SB])

        s_ids = sem("s_ids")
        s_dense = sem("s_dense")
        s_tab = [sem(f"s_tab{x}") for x in range(NX)]
        s_w = sem("s_w")
        s_zero = sem("s_zero")
        s_ident = sem("s_ident")
        s_rowno = sem("s_rowno")
        s_pad = sem("s_pad")
        s_hi = sem("s_hi")
        s_lo = sem("s_lo")
        s_w1 = sem("s_w1")
        s_w1sum = sem("s_w1sum")
        s_w1hi = sem("s_w1hi")
        s_w1lo = sem("s_w1lo")
        s_go = sem("s_go")
        s_sp = sem("s_sp")
        s_staged = sem("s_staged")
        s_idrow = sem("s_idrow")
        s_block = sem("s_block")
        s_oh = sem("s_oh")
        s_ohused = sem("s_ohused")
        s_gath = [[sem(f"s_gath{t}_{k}") for k in range(NB)] for t in range(TS)]
        s_dt = sem("s_dt")
        s_dcopy = sem("s_dcopy")
        s_dvec = sem("s_dvec")
        s_rows = sem("s_rows")
        s_copied = {"act": sem("s_vact"), "dve": sem("s_vdve")}
        s_gram = sem("s_gram")
        s_gact = sem("s_gact")
        s_gdve = sem("s_gdve")
        s_z = [sem(f"s_z{c}") for c in range(NZ)]
        s_zpool = [sem(f"s_zpool{c}") for c in range(NZ)]
        s_zhi = sem("s_zhi")
        s_zlo = sem("s_zlo")
        s_h1 = sem("s_h1")
        s_h1act = sem("s_h1act")
        s_h1dve = sem("s_h1dve")
        s_h2 = sem("s_h2")
        s_h2act = sem("s_h2act")
        s_y = sem("s_y")
        s_ycopy = sem("s_ycopy")
        s_yt = sem("s_yt")
        s_yready = sem("s_yready")
        s_out = sem("s_out")

        NI = len(ITEMS)
        ZMOVED = [16 * sum(b[2] == c for b in BLOCKS) for c in range(NZ)]
        WEIGHTS = 4

        def h_out(n):
            return ps_g[n // 2][:, n % 2, 0:SB]

        def pair_views(b):
            first, width, chunk, row = b
            n = F - first
            return (z[row:row + n * width, 1 + chunk, :],
                    gram[1 + first:V, first:first + width].rearrange("v c q j -> v c (q j)"))

        BY_POOL = BLOCKS[1::3]
        BY_SP = [b for b in BLOCKS if b not in BY_POOL]

        block = ctx.enter_context(nc.Block())

        @block.sync
        def _(sp):
            for q in range(Q):
                sp.dma_start(ids_all[32 * q:32 * q + 32],
                             ids.rearrange("(q n j) f -> q j n f", q=Q, j=JJ)[q]).then_inc(s_ids, 16)

            def load_ids(i):
                sp.dma_start(ids_row[:].rearrange("p x s -> p (x s)"),
                             ids_steps[i, :].partition_broadcast(P)).then_inc(s_idrow, 16)

            for x in range(NX):
                if x == 1:
                    load_ids(0)
                if x >= NSTAGE:
                    sp.wait_ge(s_lo, x - NSTAGE + 1)
                sp.dma_start(staged[0:PK, x % NSTAGE, :],
                             tables[LOOKED[x]].rearrange("(p k) d -> p (k d)", k=NK)).then_inc(s_tab[x], 16)
            for q in range(Q):
                sp.dma_start(dense_all[32 * q:32 * q + 32],
                             dense.rearrange("(q n j) d -> q j n d", q=Q, j=JJ)[q]).then_inc(s_dense, 16)
            sp.dma_start(w2s[:], w2.rearrange("(c p) n -> p c n", p=P)).then_inc(s_w, 16)
            sp.wait_ge(s_dt, NT // 4)
            sp.dma_start(w1raw, w1[:, 0:1 + NZ, :]).then_inc(s_w1, 16)
            sp.dma_start(w1second, w1[:, 1 + NZ, :]).then_inc(s_w1, 16)

            def move_pairs(i, first=False, last=False):
                if not first:
                    sp.wait_ge(s_h1, i * 2)
                    sp.sem_inc(s_sp, 1)
                sp.wait_ge(s_gact, (i + 1) * HC)
                sp.wait_ge(s_gdve, (i + 1) * HC)
                for b in BY_SP if last else BLOCKS:
                    sp.dma_start(*pair_views(b)).then_inc(s_z[b[2]], 16)

            def step(i, first=False, last=False):
                if not last:
                    sp.wait_ge(s_oh, i * HS + HS)
                    sp.sem_inc(s_sp, 1)
                    load_ids(i + 1)
                move_pairs(i, first, last)

            step(0, first=True)
            with sp.Fori(1, NS - 1) as i:
                step(i)
            step(NS - 1, last=True)
            sp.wait_ge(s_yready, 1)
            for half in range(2):
                sp.dma_start(out.rearrange("(h q i s) o -> h i q (s o)", h=2, q=Q // 2, i=NS)[half],
                             y_t[half * NS:(half + 1) * NS].rearrange("i (q s) -> i q s", q=Q // 2)
                             ).then_inc(s_out, 16)
            sp.wait_ge(s_out, 16 * 2)

        @block.gpsimd
        def _(pool):
            nc.gpsimd.memset(ident[:], 0.0).then_inc(s_zero, 1)
            pool.wait_ge(s_zero, 1)
            nc.gpsimd.affine_select(out=ident[:], in_=ident[:], compare_op=ALU.not_equal, fill=1.0, base=0,
                                    pattern=[[-1, P]], channel_multiplier=1).then_inc(s_ident, 1)
            nc.gpsimd.iota(minus_row[:], pattern=[[0, 1]], base=0, channel_multiplier=-NK).then_inc(s_rowno, 1)

            with pool.Fori(0, NS) as i:
                for t in range(TS):
                    pool.wait_ge(s_staged, i * TS + t + 1)
                    pool.sem_inc(s_go, 1)
                    for k in range(NB):
                        for f in BATCH[k]:
                            pool.indirect_dma_start(
                                out=rows[:, t, SLOT[f], :], out_offset=None, in_=tables[f],
                                in_offset=bass.IndirectOffsetOnAxis(ap=ids_cur[:, t, f:f + 1], axis=0),
                            ).then_inc(s_gath[t][k], 16)

            pool.wait_ge(s_h1, 2 * (NS - 1))
            pool.wait_ge(s_gact, NS * HC)
            pool.wait_ge(s_gdve, NS * HC)
            for b in BY_POOL:
                pool.dma_start(*pair_views(b)).then_inc(s_zpool[b[2]], 16)

        @block.tensor
        def _(pe):
            pe.wait_ge(s_ident, 1)

            def transpose_dense():
                pe.wait_ge(s_dense, 16 * Q)
                pe.wait_ge(s_copied["act"], NP)
                for g in range(NT // 4):
                    if g >= 2:
                        pe.wait_ge(s_dcopy, g - 1)
                    for n in range(4):
                        last = nc.tensor.transpose(ps_t[g % 2][:, n, :], dense_all[:, 4 * g + n, :], ident[:])
                    last.then_inc(s_dt, 1)
                pe.wait_ge(s_dcopy, NT // 4)

            def bank_free(i, m, first):
                before = [n for n in range(m) if BANK[n] == BANK[m]]
                if before:
                    e, n = COPIER[before[-1]], before[-1]
                    pe.wait_ge(s_copied[e], i * copied_by(e, NI) + copied_by(e, n + 1))
                elif not first:
                    n = max(n for n in range(NI) if BANK[n] == BANK[m])
                    e = COPIER[n]
                    pe.wait_ge(s_copied[e], i * copied_by(e, NI) - copied_by(e, NI) + copied_by(e, n + 1))

            def transposes(i, t, first):
                for k in range(NB):
                    m = ITEMS.index(("rows", t, k))
                    batch = BATCH[k]
                    pe.wait_ge(s_gath[t][k], (i + 1) * (16 * len(batch)))
                    bank_free(i, m, first)
                    for n, f in enumerate(batch):
                        last = nc.tensor.transpose(ps_t[BANK[m]][:, n, :], rows[:, t, SLOT[f], :], ident[:])
                    last.then_inc(s_rows, 1)

            def lookups(i, first):
                for x in range(0, NX, 2):
                    m = ITEMS.index(("lookup", None, x))
                    bank_free(i, m, first)
                    for n in range(min(2, NX - x)):
                        if first:
                            pe.wait_ge(s_hi, x + n + 1)
                            pe.wait_ge(s_lo, x + n + 1)
                        o = ps_t[BANK[m]][:, 2 * n:2 * n + 2, :]
                        for part in range(NO):
                            h = NO * (x + n) + part
                            pe.wait_ge(s_oh, i * HS + h + 1)
                            for k in range(HK):
                                b = part * HK + k
                                for tab in (tab_hi, tab_lo):
                                    last = nc.tensor.matmul(
                                        o, tab[0:PK, x + n, b, :], onehot[0:PK, part, k, :],
                                        start=(b == 0 and tab is tab_hi),
                                        stop=(b == NK - 1 and tab is tab_lo))
                            last.then_inc(s_ohused, 1)

            def gram_products(i, t, first):
                m = TILE_READY[t]
                for e in ("act", "dve"):
                    pe.wait_ge(s_copied[e], i * copied_by(e, NI) + copied_by(e, m))
                pe.wait_ge(s_dvec, i * TS + t + 1)
                if t == 0 and not first:
                    pe.wait_ge(s_h1act, i * 1)
                if first and t == 0:
                    pe.wait_ge(s_pad, 1)
                for c in range(NC):
                    g = NC * t + c
                    if g == 1 and not first:
                        pe.wait_ge(s_h1dve, i * 1)
                    if g >= 2 or not first:
                        pe.wait_ge(s_gdve if g % 2 else s_gact, i * HC + g // 2)
                    for n in range(CH):
                        jj = CH * c + n
                        last = nc.tensor.matmul(
                            ps_g[g % 2][:, n // GB, (n % GB) * Q * GC:(n % GB + 1) * Q * GC],
                            vec_t[:, t, jj].rearrange("p q v -> p (q v)"), vec_t[:, t, jj, :, 0:GC],
                            start=True, stop=True)
                    last.then_inc(s_gram, 1)

            def layer_one(i, last=False):
                if last:
                    pe.wait_ge(s_gact, NS * HC)
                    pe.wait_ge(s_gdve, NS * HC)
                for c in range(1 + NZ):
                    r = ZR if c else D
                    pe.wait_ge(s_zlo, i * (1 + NZ) + c + 1)
                    for n in range(N1 // P):
                        cols = slice(n * P, (n + 1) * P)
                        for w, x in ((w1_hi, z_hi), (w1_hi, z_lo), (w1_lo, z_hi)):
                            done = nc.tensor.matmul(h_out(n), w[0:r, c, cols], x[0:r, c, :],
                                                    start=(c == 0 and w is w1_hi and x is z_hi),
                                                    stop=(c == NZ and w is w1_lo))
                        if c == NZ and n % 2:
                            done.then_inc(s_h1, 1)

            def layer_two(i, first=False):
                pe.wait_ge(s_h1act, i + 1)
                pe.wait_ge(s_h1dve, i + 1)
                if not first:
                    pe.wait_ge(s_ycopy, i * 1)
                for n in range(N2 // P):
                    for c in range(N1 // P):
                        last = nc.tensor.matmul(ps_h[:, n, :], w2s[:, c, n * P:(n + 1) * P], h1[:, c, :],
                                                start=(c == 0), stop=(c == N1 // P - 1))
                last.then_inc(s_h2, 1)

            def layer_three(i):
                pe.wait_ge(s_h2act, i + 1)
                for half in range(2):
                    for c in range(N2 // P):
                        last = nc.tensor.matmul(ps_h[:, 0, half:half + 1], h2[:, c, half * P:(half + 1) * P],
                                                w3s[:, c:c + 1], start=(c == 0), stop=(c == N2 // P - 1))
                last.then_inc(s_y, 1)

            def step(i, second=False):
                lookups(i, False)
                transposes(i, 0, False)
                layer_one(i - 1)
                transposes(i, 1, False)
                gram_products(i, 0, False)
                layer_two(i - 1, first=second)
                gram_products(i, 1, False)
                layer_three(i - 1)

            lookups(0, True)
            transpose_dense()
            for t in range(TS):
                transposes(0, t, True)
                gram_products(0, t, True)
            pe.wait_ge(s_w, 16 * WEIGHTS)
            pe.wait_ge(s_w1lo, 1)
            step(1, second=True)
            with pe.Fori(2, NS) as i:
                step(i)
            layer_one(NS - 1, last=True)
            layer_two(NS - 1)
            layer_three(NS - 1)
            pe.wait_ge(s_ycopy, NS)
            nc.tensor.transpose(ps_t[0][0:2 * NS, 0, :], y[:].rearrange("p h i -> p (h i)"),
                                ident[:]).then_inc(s_yt, 1)

        def copy_gram(engine_copy, t, c, done):
            g = NC * t + c
            for q in range(Q):
                src = ps_g[g % 2][32 * q:32 * q + 32, :, 0:GB * Q * GC].rearrange(
                    "v b (n c) -> v b n c", n=GB)[:, :, :, GC * q:GC * (q + 1)].rearrange("v b n c -> v c b n")
                at = JJ * t + CH * c
                dst = gram[0:32, :, q, at:at + CH].rearrange("v c (b n) -> v c b n", b=2)
                last = engine_copy(dst, src)
            last.then_inc(done, 1)

        def item_views(m):
            kind, t, k = ITEMS[m]
            bank = ps_t[BANK[m]]
            if kind == "rows":
                at = 0
                for lo, hi in GATHERED[k]:
                    yield (vec_t[:, t, :, :, 1 + lo:1 + hi].rearrange("p j q f -> p f q j"),
                           bank[:, at:at + hi - lo, :].rearrange("p f (q j) -> p f q j", q=Q))
                    at += hi - lo
            else:
                f, n = LOOKED[k], min(2, NX - k)
                yield (vec_t[:].rearrange("p t j q v -> p (t j) q v")[:, :, :, 1 + f:1 + f + n].rearrange(
                           "p j q f -> p f q j"),
                       bank[:, 0:n * TS, :].rearrange("p (f h) s -> p f (h s)", f=n).rearrange(
                           "p f (q j) -> p f q j", q=Q))

        def copy_items(engine, eng, copy, i, kind, t, batches=range(NI)):
            for m in range(NI):
                if ITEMS[m][:2] == (kind, t) and COPIER[m] == engine and ITEMS[m][2] in batches:
                    if kind == "rows":
                        eng.wait_ge(s_rows, i * (TS * NB) + NB * t + ITEMS[m][2] + 1)
                    else:
                        eng.wait_ge(s_ohused, i * HS + NO * min(ITEMS[m][2] + 2, NX))
                    for views in item_views(m):
                        last = copy(*views)
                    last.then_inc(s_copied[engine], 1)

        @block.scalar
        def _(act):
            act.dma_start(b1s[:], b1).then_inc(s_w, 16)
            act.dma_start(b2s[:], b2).then_inc(s_w, 16)
            act.dma_start(w3s[:], w3).then_inc(s_w, 16)
            act.wait_ge(s_rowno, 2)
            for x in range(NX):
                if x == 1:
                    act.wait_ge(s_idrow, 16)
                    nc.scalar.activation(block_no[0:PK], ids_row[0:PK], ACT.Identity,
                                         bias=minus_rowf[0:PK, 0:1]).then_inc(s_block, 1)
                act.wait_ge(s_tab[x], 16)
                nc.scalar.copy(tab_hi[0:PK, x].rearrange("p k d -> p (k d)"),
                               staged[0:PK, x % NSTAGE, :]).then_inc(s_hi, 1)

            def number_blocks(i):
                act.wait_ge(s_idrow, i * 16 + 16)
                nc.scalar.activation(block_no[0:PK], ids_row[0:PK], ACT.Identity,
                                     bias=minus_rowf[0:PK, 0:1]).then_inc(s_block, 1)

            def copy_chunks(i, t):
                for c in range(0, NC, 2):
                    act.wait_ge(s_gram, i * CS + NC * t + c + 1)
                    copy_gram(nc.scalar.copy, t, c, s_gact)

            def relu_one(i):
                act.wait_ge(s_h1, i * 2 + 1)
                for n in range(2):
                    done = nc.scalar.activation(h1[:, n, :], h_out(n), ACT.Relu, bias=b1s[:, n:n + 1])
                done.then_inc(s_h1act, 1)

            def relu_two(i):
                act.wait_ge(s_h2, i + 1)
                for n in range(N2 // P):
                    last = nc.scalar.activation(h2[:, n, :], ps_h[:, n, :], ACT.Relu, bias=b2s[:, n:n + 1])
                last.then_inc(s_h2act, 1)

            def copy_y(i):
                act.wait_ge(s_y, i + 1)
                nc.scalar.copy(y[:, :, bass.ds(i, 1)].rearrange("p h i -> p (h i)"),
                               ps_h[:, 0, 0:2]).then_inc(s_ycopy, 1)

            def split_z(i, last=False):
                act.wait_ge(s_h1, i * 2)
                nc.scalar.copy(z_hi[:, 0, :].rearrange("p (q j) -> p q j", q=Q),
                               dense_t[:, :, bass.ds(i * SJ, SJ)]).then_inc(s_zhi, 1)
                for c in range(NZ):
                    if last:
                        act.wait_ge(s_z[c], (NS - 1) * ZMOVED[c] + 16 * sum(b[2] == c for b in BY_SP))
                        act.wait_ge(s_zpool[c], 16 * sum(b[2] == c for b in BY_POOL))
                    else:
                        act.wait_ge(s_z[c], (i + 1) * ZMOVED[c])
                    nc.scalar.copy(z_hi[0:ZR, 1 + c, :], z[0:ZR, 1 + c, :]).then_inc(s_zhi, 1)

            def step(i, last=False):
                copy_items("act", act, nc.scalar.copy, i, "lookup", None, range(NX - 1))
                split_z(i - 1)
                copy_items("act", act, nc.scalar.copy, i, "lookup", None, range(NX - 1, NX))
                copy_items("act", act, nc.scalar.copy, i, "rows", 0)
                relu_one(i - 1)
                copy_items("act", act, nc.scalar.copy, i, "rows", 1)
                if not last:
                    number_blocks(i + 1)
                copy_chunks(i, 0)
                relu_two(i - 1)
                copy_chunks(i, 1)
                copy_y(i - 1)

            copy_items("act", act, nc.scalar.copy, 0, "lookup", None)
            for t in range(TS):
                copy_items("act", act, nc.scalar.copy, 0, "rows", t)
                copy_chunks(0, t)
            number_blocks(1)
            act.wait_ge(s_w1sum, 1)
            nc.scalar.copy(w1_hi[:], w1raw).then_inc(s_w1hi, 1)
            act.wait_ge(s_w, 16 * WEIGHTS)
            step(1)
            with act.Fori(2, NS - 1) as i:
                step(i)
            step(NS - 1, last=True)
            split_z(NS - 1, last=True)
            relu_one(NS - 1)
            relu_two(NS - 1)
            copy_y(NS - 1)
            act.wait_ge(s_yt, 1)
            nc.scalar.copy(y_t[:], ps_t[0][0:2 * NS, 0, :]).then_inc(s_yready, 1)

        @block.vector
        def _(dve):
            nc.vector.memset(vec_t[:, :, :, :, V:], 0.0).then_inc(s_pad, 1)
            nc.vector.memset(z[96:P, 1:, :], 0.0).then_inc(s_pad, 1)
            dve.wait_ge(s_rowno, 1)
            nc.vector.tensor_copy(minus_rowf[:], minus_row[:]).then_inc(s_rowno, 1)
            dve.wait_ge(s_ids, 16 * Q)
            for t in range(TS):
                nc.vector.tensor_copy(ids_cur[:, t, :], ids_all[:, t, :]).then_inc(s_staged, 1)
            def make_onehot(i, parts, first):
                for h in parts:
                    if h == 0:
                        dve.wait_ge(s_block, i + 1)
                    if h >= NO or not first:
                        dve.wait_ge(s_ohused, i * HS + h - NO + 1)
                    for k in range(HK):
                        last = nc.vector.tensor_scalar(onehot[0:PK, h % NO, k, :], block_no[0:PK, h // NO, :],
                                                       float((h % NO) * HK + k), None, ALU.is_equal)
                    last.then_inc(s_oh, 1)

            def put_dense(i, t, first):
                if not first:
                    dve.wait_ge(s_gram, i * CS - CS + NC * (t + 1))
                nc.vector.tensor_copy(vec_t[:, t, :, :, 0].rearrange("p j q -> p q j"),
                                      dense_t[:, :, bass.ds(i * SJ + t * JJ, JJ)]).then_inc(s_dvec, 1)

            def stage_ids(i, t):
                dve.wait_ge(s_rows, i * (TS * NB) + NB * (t + 1))
                nc.vector.tensor_copy(ids_cur[:, t, :], ids_all[:, bass.ds(i * TS + TS + t, 1), :]
                                      .rearrange("p o f -> p (o f)")).then_inc(s_staged, 1)

            def copy_chunks(i, t):
                for c in range(1, NC, 2):
                    dve.wait_ge(s_gram, i * CS + NC * t + c + 1)
                    copy_gram(nc.vector.tensor_copy, t, c, s_gdve)

            def relu_one(i):
                dve.wait_ge(s_h1, i * 2 + 2)
                for n in range(2, 4):
                    done = nc.vector.tensor_scalar(h1[:, n, :], h_out(n), b1s[:, n:n + 1], 0.0,
                                                   ALU.add, ALU.max)
                done.then_inc(s_h1dve, 1)

            def split_z(i):
                dve.wait_ge(s_zhi, i * (1 + NZ) + 1)
                nc.vector.tensor_sub(z_lo[:, 0, :].rearrange("p (q j) -> p q j", q=Q),
                                     dense_t[:, :, bass.ds(i * SJ, SJ)],
                                     z_hi[:, 0, :].bitcast(fp32).rearrange("p (q j) -> p q j", q=Q)
                                     ).then_inc(s_zlo, 1)
                for c in range(1, 1 + NZ):
                    dve.wait_ge(s_zhi, i * (1 + NZ) + c + 1)
                    nc.vector.tensor_sub(z_lo[0:ZR, c, :], z[0:ZR, c, :],
                                         z_hi[0:ZR, c, :].bitcast(fp32)).then_inc(s_zlo, 1)

            def step(i, last=False):
                make_onehot(i, range(NO, HS), False)
                split_z(i - 1)
                for t in range(TS):
                    put_dense(i, t, False)
                for t in range(TS):
                    if t == 1:
                        relu_one(i - 1)
                    copy_items("dve", dve, nc.vector.tensor_copy, i, "rows", t)
                    if not last:
                        stage_ids(i, t)
                copy_chunks(i, 0)
                if not last:
                    make_onehot(i + 1, range(NO), False)
                copy_chunks(i, 1)

            def split_low(x):
                dve.wait_ge(s_hi, x + 1)
                nc.vector.tensor_sub(tab_lo[0:PK, x].rearrange("p k d -> p (k d)"),
                                     staged[0:PK, x % NSTAGE, :],
                                     tab_hi[0:PK, x].rearrange("p k d -> p (k d)").bitcast(fp32)).then_inc(s_lo, 1)

            split_low(0)
            make_onehot(0, range(NO), True)
            for x in range(1, NX):
                split_low(x)
                make_onehot(0, range(NO * x, NO * (x + 1)), True)
            for g in range(NT // 4):
                dve.wait_ge(s_dt, g + 1)
                nc.vector.tensor_copy(
                    dense_t[:, :, g * 4 * JJ:(g + 1) * 4 * JJ].rearrange("p q (n j) -> p n q j", n=4),
                    ps_t[g % 2][:].rearrange("p n (q j) -> p n q j", q=Q)).then_inc(s_dcopy, 1)
            dve.wait_ge(s_dcopy, NT // 4)
            for t in range(TS):
                put_dense(0, t, True)
            for t in range(TS):
                copy_items("dve", dve, nc.vector.tensor_copy, 0, "rows", t)
                stage_ids(0, t)
                copy_chunks(0, t)
            make_onehot(1, range(NO), False)
            dve.wait_ge(s_w1, 16 * 2)
            nc.vector.tensor_add(w1raw[:, 0, :], w1raw[:, 0, :], w1second).then_inc(s_w1sum, 1)
            dve.wait_ge(s_w1hi, 1)
            nc.vector.tensor_sub(w1_lo[:], w1raw, w1_hi[:].bitcast(fp32)).then_inc(s_w1lo, 1)
            dve.wait_ge(s_w, 16 * WEIGHTS)
            with dve.Fori(1, NS - 1) as i:
                step(i)
            step(NS - 1, last=True)
            split_z(NS - 1)
            relu_one(NS - 1)


_TABLES = [f"tbl_{f}" for f in range(F)]
_INS = ["r_dense_features", "ids", *_TABLES, "b_top1", "W_top2", "b_top2", "W_top3"]
_COLUMNS = ["b_top1", "b_top2", "W_top3"]


def kernel(**inputs):
    import numpy as np
    import concourse.bacc as bacc
    from concourse.bass_utils import run_bass_kernel_spmd as run

    nc = bacc.Bacc("TRN2", target_bir_lowering=False, num_devices=1)
    arrays, a = {}, {}

    def give(name, x):
        x = np.ascontiguousarray(x)
        arrays[f"in_{name}"] = x
        a[name] = nc.dram_tensor(f"in_{name}", x.shape, mybir.dt.from_np(x.dtype), kind="ExternalInput").ap()

    for name in _INS:
        x = np.asarray(inputs[name])
        if name in _COLUMNS:
            x = x.reshape(-1, P).T
        give(name, x)
    w = np.asarray(inputs["W_top1"])
    zeros = np.zeros((1, N1), w.dtype)
    chunks = [w[0:D]] + [np.concatenate([zeros if r is None else w[r:r + 1] for r in rows]) for rows in pair_rows()]
    give("W_top1", np.stack(chunks + [w[D + NPAIR:]], axis=1))
    ids = np.asarray(inputs["ids"])[:, list(LOOKED)].reshape(Q, NS, SJ, NX)
    give("ids_steps", ids.transpose(1, 3, 0, 2).reshape(NS, NX * SB))
    out = nc.dram_tensor("out_y", (B, 1), fp32, kind="ExternalOutput").ap()
    build(nc, a["r_dense_features"], a["ids"], a["ids_steps"], [a[t] for t in _TABLES], a["W_top1"],
          a["b_top1"], a["W_top2"], a["b_top2"], a["W_top3"], out)
    r = run(nc, [arrays], core_ids=[0])
    return r.results[0]["out_y"]
```

```python
from contextlib import ExitStack

import concourse.bass as bass
from concourse import mybir

B = 2048
F = 26
D = 128
P = 128
Q = 4
JJ = P // Q
NT = B // P
TS = 2
NS = NT // TS
SB = TS * P
SJ = TS * JJ
V = F + 1
GC = F
GM = 3 * 32 + F
GB = 4
CH = 2 * GB
NC = JJ // CH
CS = TS * NC
HC = CS // 2
N1, N2 = 512, 256
NPAIR = F + F * (F - 1) // 2

LOOKED = (20, 21, 22, 23, 24, 25, 2)
VS = 1000
NK = 8
PK = VS // NK
NO = 4
HK = NK // NO
NX = len(LOOKED)
HS = NO * NX
GATHERED = [[(3, 7)], [(7, 11)], [(11, 15)], [(15, 19)], [(0, 2), (19, 20)]]
NB = len(GATHERED)
BATCH = [[f for run in runs for f in range(*run)] for runs in GATHERED]
SLOT = {f: n for n, f in enumerate(f for b in BATCH for f in b)}

ITEMS = ([("lookup", None, x) for x in range(0, NX - 1, 2)] + [("rows", 0, k) for k in range(NB)]
         + [("lookup", None, NX - 1)] + [("rows", 1, k) for k in range(NB)])
NP = NX // 2
COPIER = (["act"] * NP + ["dve", "act", "dve", "act", "act"]
          + ["act"] + ["act", "act", "dve", "dve", "act"])
BANK = [m % 3 for m in range(len(ITEMS))]
TILE_READY = [NP + NB + 1, len(ITEMS)]

fp32 = mybir.dt.float32
fp32r = mybir.dt.float32r
int32 = mybir.dt.int32
ALU = mybir.AluOpType
ACT = mybir.ActivationFunctionType


def copied_by(engine, m):
    return COPIER[:m].count(engine)


NZ = 3
BLOCKS, ZR = [], []
for _chunk, _rects in enumerate((((8, 4), (12, 4)), ((2, 3), (0, 2), (24, 2)), ((5, 3), (16, 4), (20, 4)))):
    _row = 0
    for _first, _width in _rects:
        BLOCKS.append((_first, _width, _chunk, _row))
        _row += (F - _first) * _width
    ZR.append(_row)
assert max(ZR) <= P and ZR[-1] < P


def pair_rows():
    start = [D]
    for c in range(GC):
        start.append(start[-1] + F - c)
    rows = [[None] * P for _ in range(NZ)]
    for first, width, chunk, row in BLOCKS:
        for v in range(first + 1, V):
            for c in range(first, first + width):
                if c < v:
                    rows[chunk][row + (v - first - 1) * width + c - first] = start[c] + v - c - 1
    return rows


def build(nc, dense, ids, ids_steps, tables, w1, w2, b2, w3, out):
    ctx = ExitStack()
    with ctx:
        def sb(name, shape, dt=fp32):
            return ctx.enter_context(nc.sbuf_tensor(name, shape, dt))

        def pb(name, shape):
            return ctx.enter_context(nc.psum_tensor(name, shape, fp32))

        def sem(name):
            return ctx.enter_context(nc.semaphore(name))

        ids_all = sb("ids_all", [P, NT, F], int32)
        ids_cur = sb("ids_cur", [P, TS, F], int32)
        ids_row = sb("ids_row", [P, NX, SB], int32)
        block_no = ids_row[:].bitcast(fp32)
        minus_row = sb("minus_row", [P, 1], int32)
        minus_rowf = sb("minus_rowf", [P, 1])
        tab_hi = sb("tab_hi", [P, NX, NK, D], fp32r)
        tab_lo = sb("tab_lo", [P, NX, NK, D], fp32r)
        onehot = sb("onehot", [P, NO, HK, SB], fp32r)
        early = sb("early", [P, (1 + NZ) * N1])
        dense_all = early[:].rearrange("p (n d) -> p n d", n=NT)
        w1raw = early[:].rearrange("p (c n) -> p c n", n=N1)
        h2 = early[:, 0:N2 // P * SB].rearrange("p (c s) -> p c s", s=SB)
        dense_t = sb("dense_t", [P, Q, NT * JJ])
        rows = sb("rows", [P, TS, len(SLOT), D])
        vec_t = sb("vec_t", [P, TS, JJ, Q, 32])
        gram = sb("gram", [P, GC, Q, SJ])
        z_hi = sb("z_hi", [P, 1 + NZ, SB], fp32r)
        z_lo = sb("z_lo", [P, 1 + NZ, SB], fp32r)
        z = z_lo[:].bitcast(fp32)
        w1_hi = sb("w1_hi", [P, 1 + NZ, N1], fp32r)
        w1_lo = sb("w1_lo", [P, 1 + NZ, N1], fp32r)
        w2_hi = sb("w2_hi", [P, N1 // P, N2], fp32r)
        w2_lo = sb("w2_lo", [P, N1 // P, N2], fp32r)
        w3s = sb("w3s", [P, N2 // P])
        b2s = sb("b2s", [P, N2 // P])
        h1_hi = sb("h1_hi", [P, N1 // P, SB], fp32r)
        h1_lo = sb("h1_lo", [P, N1 // P, SB], fp32r)
        y = sb("y", [P, 2, NS])
        y_t = sb("y_t", [2 * NS, P])
        ident = sb("ident", [P, P])
        NSTAGE = (GC * SB - N1) // (NK * D)
        before = gram[:].rearrange("p c q j -> p (c q j)")
        staged = before[:, 0:NSTAGE * NK * D].rearrange("p (n e) -> p n e", n=NSTAGE)
        w1second = before[:, NSTAGE * NK * D:NSTAGE * NK * D + N1]
        assert N1 // P * N2 == NK * D

        ps_t = [pb(f"ps_t{i}", [P, 4, P]) for i in range(3)]
        ps_g = [pb(f"ps_g{i}", [P, 2, 512]) for i in range(2)]
        ps_h = pb("ps_h", [P, 2, SB])
        ps_h4 = ps_h[:].rearrange("p n (h s) -> p (n h) s", s=P)

        s_ids = sem("s_ids")
        s_dense = sem("s_dense")
        s_tab = [sem(f"s_tab{x}") for x in range(NX + 1)]
        s_w = sem("s_w")
        s_zero = sem("s_zero")
        s_ident = sem("s_ident")
        s_rowno = sem("s_rowno")
        s_pad = sem("s_pad")
        s_hi = sem("s_hi")
        s_lo = sem("s_lo")
        s_w1 = sem("s_w1")
        s_w1sum = sem("s_w1sum")
        s_w1hi = sem("s_w1hi")
        s_w1lo = sem("s_w1lo")
        s_go = sem("s_go")
        s_sp = sem("s_sp")
        s_staged = sem("s_staged")
        s_idfirst = sem("s_idfirst")
        s_idrow = sem("s_idrow")
        s_blockfirst = sem("s_blockfirst")
        s_block = sem("s_block")
        s_oh = sem("s_oh")
        s_ohused = sem("s_ohused")
        s_gath = [[sem(f"s_gath{t}_{k}") for k in range(NB)] for t in range(TS)]
        s_dt = sem("s_dt")
        s_dcopy = sem("s_dcopy")
        s_dvec = sem("s_dvec")
        s_rows = sem("s_rows")
        s_copied = {"act": sem("s_vact"), "dve": sem("s_vdve")}
        s_gram = sem("s_gram")
        s_gact = sem("s_gact")
        s_gdve = sem("s_gdve")
        s_z = [sem(f"s_z{c}") for c in range(NZ)]
        s_zpool = [sem(f"s_zpool{c}") for c in range(NZ)]
        s_zhi = sem("s_zhi")
        s_zlo = sem("s_zlo")
        s_h1 = sem("s_h1")
        s_h1hi = sem("s_h1hi")
        s_h1lo = sem("s_h1lo")
        s_h2 = sem("s_h2")
        s_h2act = sem("s_h2act")
        s_y = sem("s_y")
        s_ycopy = sem("s_ycopy")
        s_yt = sem("s_yt")
        s_yready = sem("s_yready")
        s_out = sem("s_out")

        NI = len(ITEMS)
        H1C = N1 // P
        ZMOVED = [16 * sum(b[2] == c for b in BLOCKS) for c in range(NZ)]

        def h_out(n):
            return ps_g[n // 2][:, n % 2, 0:SB]

        def dense_out(g):
            return ps_g[g // 2][:, g % 2, :].rearrange("p (n s) -> p n s", n=4)

        def pair_views(b):
            first, width, chunk, row = b
            n = F - first
            return (z[row:row + n * width, 1 + chunk, :],
                    gram[first:F, first:first + width].rearrange("v c q j -> v c (q j)"))

        BY_POOL = BLOCKS[1::3]
        BY_SP = [b for b in BLOCKS if b not in BY_POOL]

        block = ctx.enter_context(nc.Block())

        @block.sync
        def _(sp):
            def load_ids(i):
                sp.dma_start(ids_row[:].rearrange("p x s -> p (x s)"),
                             ids_steps[i, :].partition_broadcast(P)).then_inc(s_idrow, 16)

            sp.dma_start(ids_all[:].rearrange("p n f -> p (n f)"), ids).then_inc(s_ids, 16)
            for x in range(NX):
                if x >= NSTAGE:
                    sp.wait_ge(s_lo, x - NSTAGE + 1)
                table = tables[LOOKED[x]].rearrange("(p k) d -> p (k d)", k=NK)
                for lo, hi in ((0, PK // 16 * 16), (PK // 16 * 16, PK)):
                    sp.dma_start(staged[lo:hi, x % NSTAGE, :], table[lo:hi]).then_inc(s_tab[x], 16)
                if x == 0:
                    for lo, hi in ((0, 1), (1, NX)):
                        sp.dma_start(ids_row[:, lo:hi, :].rearrange("p x s -> p (x s)"),
                                     ids_steps[0, lo * SB:hi * SB].partition_broadcast(P)
                                     ).then_inc(s_idrow if lo else s_idfirst, 16)
                if x == 2:
                    for q in range(Q):
                        sp.dma_start(dense_all[32 * q:32 * q + 32],
                                     dense.rearrange("(q n j) d -> q j n d", q=Q, j=JJ)[q]).then_inc(s_dense, 16)
            sp.dma_start(b2s[:], b2).then_inc(s_w, 16)
            sp.dma_start(w3s[:], w3).then_inc(s_w, 16)
            sp.wait_ge(s_lo, NX - NSTAGE + 1)
            sp.dma_start(staged[:, NX % NSTAGE, :].rearrange("p (c n) -> p c n", n=N2),
                         w2.rearrange("(c p) n -> p c n", p=P)).then_inc(s_tab[NX], 16)
            sp.wait_ge(s_dt, NT // 4)
            sp.dma_start(w1raw, w1[:, 0:1 + NZ, :]).then_inc(s_w1, 16)
            sp.dma_start(w1second, w1[:, 1 + NZ, :]).then_inc(s_w1, 16)

            def move_pairs(i, first=False, last=False):
                if not first:
                    sp.wait_ge(s_h1, i * H1C)
                    sp.sem_inc(s_sp, 1)
                sp.wait_ge(s_gact, (i + 1) * HC)
                sp.wait_ge(s_gdve, (i + 1) * HC)
                for b in BY_SP if last else BLOCKS:
                    sp.dma_start(*pair_views(b)).then_inc(s_z[b[2]], 16)

            def step(i, first=False, last=False):
                if not last:
                    sp.wait_ge(s_oh, i * HS + HS)
                    sp.sem_inc(s_sp, 1)
                    load_ids(i + 1)
                move_pairs(i, first, last)

            step(0, first=True)
            with sp.Fori(1, NS - 1) as i:
                step(i)
            step(NS - 1, last=True)
            sp.wait_ge(s_yready, 1)
            for half in range(2):
                sp.dma_start(out.rearrange("(h q i s) o -> h i q (s o)", h=2, q=Q // 2, i=NS)[half],
                             y_t[half * NS:(half + 1) * NS].rearrange("i (q s) -> i q s", q=Q // 2)
                             ).then_inc(s_out, 16)
            sp.wait_ge(s_out, 16 * 2)

        @block.gpsimd
        def _(pool):
            nc.gpsimd.memset(ident[:], 0.0).then_inc(s_zero, 1)
            pool.wait_ge(s_zero, 1)
            nc.gpsimd.affine_select(out=ident[:], in_=ident[:], compare_op=ALU.not_equal, fill=1.0, base=0,
                                    pattern=[[-1, P]], channel_multiplier=1).then_inc(s_ident, 1)
            nc.gpsimd.iota(minus_row[:], pattern=[[0, 1]], base=0, channel_multiplier=-NK).then_inc(s_rowno, 1)

            with pool.Fori(0, NS) as i:
                for t in range(TS):
                    pool.wait_ge(s_staged, i * TS + t + 1)
                    pool.sem_inc(s_go, 1)
                    for k in range(NB):
                        for f in BATCH[k]:
                            pool.indirect_dma_start(
                                out=rows[:, t, SLOT[f], :], out_offset=None, in_=tables[f],
                                in_offset=bass.IndirectOffsetOnAxis(ap=ids_cur[:, t, f:f + 1], axis=0),
                            ).then_inc(s_gath[t][k], 16)

            pool.wait_ge(s_h1, H1C * (NS - 1))
            pool.wait_ge(s_gact, NS * HC)
            pool.wait_ge(s_gdve, NS * HC)
            for b in BY_POOL:
                pool.dma_start(*pair_views(b)).then_inc(s_zpool[b[2]], 16)

        @block.tensor
        def _(pe):
            pe.wait_ge(s_ident, 1)

            def transpose_dense():
                pe.wait_ge(s_dense, 16 * Q)
                for g in range(NT // 4):
                    for n in range(4):
                        last = nc.tensor.transpose(dense_out(g)[:, n, :], dense_all[:, 4 * g + n, :], ident[:])
                    last.then_inc(s_dt, 1)

            def bank_free(i, m, first):
                before = [n for n in range(m) if BANK[n] == BANK[m]]
                if before:
                    e, n = COPIER[before[-1]], before[-1]
                    pe.wait_ge(s_copied[e], i * copied_by(e, NI) + copied_by(e, n + 1))
                elif not first:
                    n = max(n for n in range(NI) if BANK[n] == BANK[m])
                    e = COPIER[n]
                    pe.wait_ge(s_copied[e], i * copied_by(e, NI) - copied_by(e, NI) + copied_by(e, n + 1))

            def transposes(i, t, first):
                for k in range(NB):
                    m = ITEMS.index(("rows", t, k))
                    batch = BATCH[k]
                    pe.wait_ge(s_gath[t][k], (i + 1) * (16 * len(batch)))
                    bank_free(i, m, first)
                    for n, f in enumerate(batch):
                        last = nc.tensor.transpose(ps_t[BANK[m]][:, n, :], rows[:, t, SLOT[f], :], ident[:])
                    last.then_inc(s_rows, 1)

            def lookups(i, first, pairs, bank=None):
                for x in pairs:
                    m = ITEMS.index(("lookup", None, x))
                    if bank is None:
                        bank_free(i, m, first)
                    for n in range(min(2, NX - x)):
                        if first:
                            pe.wait_ge(s_hi, x + n + 1)
                            pe.wait_ge(s_lo, x + n + 1)
                        o = (ps_t[BANK[m]] if bank is None else bank)[:, 2 * n:2 * n + 2, :]
                        for part in range(NO):
                            h = NO * (x + n) + part
                            pe.wait_ge(s_oh, i * HS + h + 1)
                            for k in range(HK):
                                b = part * HK + k
                                for tab in (tab_hi, tab_lo):
                                    last = nc.tensor.matmul(
                                        o, tab[0:PK, x + n, b, :], onehot[0:PK, part, k, :],
                                        start=(b == 0 and tab is tab_hi),
                                        stop=(b == NK - 1 and tab is tab_lo))
                            last.then_inc(s_ohused, 1)

            def gram_products(i, t, first):
                m = TILE_READY[t]
                for e in ("act", "dve"):
                    pe.wait_ge(s_copied[e], i * copied_by(e, NI) + copied_by(e, m))
                pe.wait_ge(s_dvec, i * TS + t + 1)
                if t == 0 and not first:
                    pe.wait_ge(s_h1lo, i * H1C - H1C + H1C // 2)
                if first and t == 0:
                    pe.wait_ge(s_pad, 1)
                for c in range(NC):
                    g = NC * t + c
                    if g == 1 and not first:
                        pe.wait_ge(s_h1lo, i * H1C)
                    if g >= 2 or not first:
                        pe.wait_ge(s_gdve if g % 2 else s_gact, i * HC + g // 2)
                    for n in range(CH):
                        jj = CH * c + n
                        last = nc.tensor.matmul(
                            ps_g[g % 2][0:GM, n // GB, (n % GB) * Q * GC:(n % GB + 1) * Q * GC],
                            vec_t[:, t, jj].rearrange("p q v -> p (q v)")[:, 1:1 + GM], vec_t[:, t, jj, :, 0:GC],
                            start=True, stop=True)
                    last.then_inc(s_gram, 1)

            def layer_one(i, last=False):
                if last:
                    pe.wait_ge(s_gact, NS * HC)
                    pe.wait_ge(s_gdve, NS * HC)
                for c in range(1 + NZ):
                    pe.wait_ge(s_zlo, i * (1 + NZ) + c + 1)
                    for n in range(N1 // P):
                        cols = slice(n * P, (n + 1) * P)
                        for w, x in ((w1_hi, z_hi), (w1_hi, z_lo), (w1_lo, z_hi)):
                            done = nc.tensor.matmul(h_out(n), w[:, c, cols], x[:, c, :],
                                                    start=(c == 0 and w is w1_hi and x is z_hi),
                                                    stop=(c == NZ and w is w1_lo))
                        if c == NZ:
                            done.then_inc(s_h1, 1)

            def layer_two(i, first=False):
                if not first:
                    pe.wait_ge(s_ycopy, i * 1)
                for n in range(N2 // P):
                    for c in range(H1C):
                        if n == 0:
                            pe.wait_ge(s_h1lo, i * H1C + c + 1)
                        cols = slice(n * P, (n + 1) * P)
                        for w, x in ((w2_hi, h1_hi), (w2_hi, h1_lo), (w2_lo, h1_hi)):
                            last = nc.tensor.matmul(ps_h[:, n, :], w[:, c, cols], x[:, c, :],
                                                    start=(c == 0 and w is w2_hi and x is h1_hi),
                                                    stop=(c == H1C - 1 and w is w2_lo))
                last.then_inc(s_h2, 1)

            def layer_three(i):
                pe.wait_ge(s_h2act, i + 1)
                for half in range(2):
                    for c in range(N2 // P):
                        last = nc.tensor.matmul(ps_h[:, 0, half:half + 1], h2[:, c, half * P:(half + 1) * P],
                                                w3s[:, c:c + 1], start=(c == 0), stop=(c == N2 // P - 1))
                last.then_inc(s_y, 1)

            PAIRS = range(0, NX - 1, 2)
            SINGLE = range(NX - 1, NX)

            def step(i, second=False):
                lookups(i, False, PAIRS[1:] if second else PAIRS)
                transposes(i, 0, False)
                if second:
                    pe.wait_ge(s_w1lo, 1)
                    pe.wait_ge(s_lo, NX + 1)
                    pe.wait_ge(s_w, 16 * 2)
                layer_one(i - 1)
                lookups(i, False, SINGLE)
                layer_two(i - 1, first=second)
                gram_products(i, 0, False)
                transposes(i, 1, False)
                layer_three(i - 1)
                gram_products(i, 1, False)

            lookups(0, True, PAIRS[:1])
            transpose_dense()
            lookups(0, True, PAIRS[1:])
            lookups(0, True, SINGLE, bank=ps_h4)
            transposes(0, 0, True)
            pe.wait_ge(s_dcopy, NT // 4)
            gram_products(0, 0, True)
            lookups(1, False, PAIRS[:1], bank=ps_h4)
            transposes(0, 1, True)
            gram_products(0, 1, True)
            step(1, second=True)
            with pe.Fori(2, NS) as i:
                step(i)
            layer_one(NS - 1, last=True)
            layer_two(NS - 1)
            layer_three(NS - 1)
            pe.wait_ge(s_ycopy, NS)
            nc.tensor.transpose(ps_t[0][0:2 * NS, 0, :], y[:].rearrange("p h i -> p (h i)"),
                                ident[:]).then_inc(s_yt, 1)

        def copy_gram(engine_copy, t, c, done):
            g = NC * t + c
            for q in range(Q):
                src = ps_g[g % 2][32 * q:32 * q + F, :, 0:GB * Q * GC].rearrange(
                    "v b (n c) -> v b n c", n=GB)[:, :, :, GC * q:GC * (q + 1)].rearrange("v b n c -> v c b n")
                at = JJ * t + CH * c
                dst = gram[0:F, :, q, at:at + CH].rearrange("v c (b n) -> v c b n", b=2)
                last = engine_copy(dst, src)
            last.then_inc(done, 1)

        def item_views(m, bank):
            kind, t, k = ITEMS[m]
            bank = ps_t[BANK[m]] if bank is None else bank
            if kind == "rows":
                at = 0
                for lo, hi in GATHERED[k]:
                    yield (vec_t[:, t, :, :, 1 + lo:1 + hi].rearrange("p j q f -> p f q j"),
                           bank[:, at:at + hi - lo, :].rearrange("p f (q j) -> p f q j", q=Q))
                    at += hi - lo
            else:
                f, n = LOOKED[k], min(2, NX - k)
                yield (vec_t[:].rearrange("p t j q v -> p (t j) q v")[:, :, :, 1 + f:1 + f + n].rearrange(
                           "p j q f -> p f q j"),
                       bank[:, 0:n * TS, :].rearrange("p (f h) s -> p f (h s)", f=n).rearrange(
                           "p f (q j) -> p f q j", q=Q))

        def copy_items(engine, eng, copy, i, kind, t, batches=range(NI), bank=None):
            for m in range(NI):
                if ITEMS[m][:2] == (kind, t) and COPIER[m] == engine and ITEMS[m][2] in batches:
                    if kind == "rows":
                        eng.wait_ge(s_rows, i * (TS * NB) + NB * t + ITEMS[m][2] + 1)
                    else:
                        eng.wait_ge(s_ohused, i * HS + NO * min(ITEMS[m][2] + 2, NX))
                    for views in item_views(m, bank):
                        last = copy(*views)
                    last.then_inc(s_copied[engine], 1)

        @block.scalar
        def _(act):
            act.wait_ge(s_rowno, 1)
            nc.scalar.copy(minus_rowf[:], minus_row[:]).then_inc(s_rowno, 1)
            act.wait_ge(s_rowno, 2)

            def split_high(x):
                act.wait_ge(s_tab[x], 16 * 2)
                nc.scalar.copy(tab_hi[0:PK, x].rearrange("p k d -> p (k d)"),
                               staged[0:PK, x % NSTAGE, :]).then_inc(s_hi, 1)

            def number_first(lo, hi):
                act.wait_ge(s_idrow if lo else s_idfirst, 16)
                nc.scalar.activation(block_no[0:PK, lo:hi], ids_row[0:PK, lo:hi], ACT.Identity,
                                     bias=minus_rowf[0:PK, 0:1]).then_inc(s_block if lo else s_blockfirst, 1)

            split_high(0)
            number_first(0, 1)
            split_high(1)
            number_first(1, NX)
            for x in range(2, NX):
                split_high(x)
                if x == 4:
                    for g in range(NT // 4):
                        act.wait_ge(s_dt, g + 1)
                        nc.scalar.copy(
                            dense_t[:, :, g * 4 * JJ:(g + 1) * 4 * JJ].rearrange("p q (n j) -> p n q j", n=4),
                            dense_out(g).rearrange("p n (q j) -> p n q j", q=Q)).then_inc(s_dcopy, 1)
            act.wait_ge(s_tab[NX], 16)
            nc.scalar.copy(w2_hi[:].rearrange("p c n -> p (c n)"),
                           staged[:, NX % NSTAGE, :]).then_inc(s_hi, 1)

            def number_blocks(i):
                act.wait_ge(s_idrow, i * 16 + 16)
                nc.scalar.activation(block_no[0:PK], ids_row[0:PK], ACT.Identity,
                                     bias=minus_rowf[0:PK, 0:1]).then_inc(s_block, 1)

            def copy_chunks(i, t, between=None):
                for c in range(0, NC, 2):
                    act.wait_ge(s_gram, i * CS + NC * t + c + 1)
                    copy_gram(nc.scalar.copy, t, c, s_gact)
                    if c == 0 and between is not None:
                        number_blocks(between)

            def relu_one(i):
                for n in range(H1C):
                    act.wait_ge(s_h1, i * H1C + n + 1)
                    nc.scalar.activation(h1_hi[:, n, :], h_out(n), ACT.Relu).then_inc(s_h1hi, 1)

            def relu_two(i):
                act.wait_ge(s_h2, i + 1)
                for n in range(N2 // P):
                    last = nc.scalar.activation(h2[:, n, :], ps_h[:, n, :], ACT.Relu, bias=b2s[:, n:n + 1])
                last.then_inc(s_h2act, 1)

            def copy_y(i):
                act.wait_ge(s_y, i + 1)
                nc.scalar.copy(y[:, :, bass.ds(i, 1)].rearrange("p h i -> p (h i)"),
                               ps_h[:, 0, 0:2]).then_inc(s_ycopy, 1)

            def split_z(i, last=False):
                act.wait_ge(s_h1, i * H1C)
                nc.scalar.copy(z_hi[:, 0, :].rearrange("p (q j) -> p q j", q=Q),
                               dense_t[:, :, bass.ds(i * SJ, SJ)]).then_inc(s_zhi, 1)
                for c in range(NZ):
                    if last:
                        act.wait_ge(s_z[c], (NS - 1) * ZMOVED[c] + 16 * sum(b[2] == c for b in BY_SP))
                        act.wait_ge(s_zpool[c], 16 * sum(b[2] == c for b in BY_POOL))
                    else:
                        act.wait_ge(s_z[c], (i + 1) * ZMOVED[c])
                    nc.scalar.copy(z_hi[0:ZR[c], 1 + c, :], z[0:ZR[c], 1 + c, :]).then_inc(s_zhi, 1)

            def lookup_copies(i, pairs, bank=None):
                copy_items("act", act, nc.scalar.copy, i, "lookup", None, pairs, bank)

            def row_copies(i, t):
                copy_items("act", act, nc.scalar.copy, i, "rows", t)

            def step(i, second=False, last=False):
                if second:
                    act.wait_ge(s_gram, CS)
                lookup_copies(i, range(1), ps_h4 if second else None)
                lookup_copies(i, range(1, 4))
                split_z(i - 1)
                lookup_copies(i, range(4, NX - 1))
                row_copies(i, 0)
                relu_one(i - 1)
                lookup_copies(i, range(NX - 1, NX))
                if second:
                    act.wait_ge(s_w, 16 * 2)
                relu_two(i - 1)
                copy_chunks(i, 0, between=None if last else i + 1)
                row_copies(i, 1)
                copy_y(i - 1)
                copy_chunks(i, 1)

            lookup_copies(0, range(NX - 1))
            row_copies(0, 0)
            lookup_copies(0, range(NX - 1, NX), ps_h4)
            number_blocks(1)
            copy_chunks(0, 0)
            row_copies(0, 1)
            act.wait_ge(s_w1sum, 1)
            nc.scalar.copy(w1_hi[:], w1raw).then_inc(s_w1hi, 1)
            copy_chunks(0, 1)
            step(1, second=True)
            with act.Fori(2, NS - 1) as i:
                step(i)
            step(NS - 1, last=True)
            split_z(NS - 1, last=True)
            relu_one(NS - 1)
            relu_two(NS - 1)
            copy_y(NS - 1)
            act.wait_ge(s_yt, 1)
            nc.scalar.copy(y_t[:], ps_t[0][0:2 * NS, 0, :]).then_inc(s_yready, 1)

        @block.vector
        def _(dve):
            dve.wait_ge(s_ids, 16)
            for t in range(TS):
                nc.vector.tensor_copy(ids_cur[:, t, :], ids_all[:, t, :]).then_inc(s_staged, 1)
            nc.vector.memset(vec_t[:, :, :, :, V:], 0.0).then_inc(s_pad, 1)
            nc.vector.memset(z_hi[96:P, NZ, :].bitcast(fp32), 1.0).then_inc(s_pad, 1)
            nc.vector.memset(z[96:P, NZ, :], 0.0).then_inc(s_pad, 1)

            def make_onehot(i, parts, first):
                for h in parts:
                    if first and h == 0:
                        dve.wait_ge(s_blockfirst, 1)
                    elif h == (NO if first else 0):
                        dve.wait_ge(s_block, i + 1)
                    if h >= NO or not first:
                        dve.wait_ge(s_ohused, i * HS + h - NO + 1)
                    for k in range(HK):
                        last = nc.vector.tensor_scalar(onehot[0:PK, h % NO, k, :], block_no[0:PK, h // NO, :],
                                                       float((h % NO) * HK + k), None, ALU.is_equal)
                    last.then_inc(s_oh, 1)

            def put_dense(i, t, first):
                if not first:
                    dve.wait_ge(s_gram, i * CS - CS + NC * (t + 1))
                nc.vector.tensor_copy(vec_t[:, t, :, :, 0].rearrange("p j q -> p q j"),
                                      dense_t[:, :, bass.ds(i * SJ + t * JJ, JJ)]).then_inc(s_dvec, 1)

            def stage_ids(i, t):
                dve.wait_ge(s_rows, i * (TS * NB) + NB * (t + 1))
                nc.vector.tensor_copy(ids_cur[:, t, :], ids_all[:, bass.ds(i * TS + TS + t, 1), :]
                                      .rearrange("p o f -> p (o f)")).then_inc(s_staged, 1)

            def copy_chunks(i, t):
                for c in range(1, NC, 2):
                    dve.wait_ge(s_gram, i * CS + NC * t + c + 1)
                    copy_gram(nc.vector.tensor_copy, t, c, s_gdve)

            def relu_one(i, chunks):
                for n in chunks:
                    dve.wait_ge(s_h1hi, i * H1C + n + 1)
                    nc.vector.scalar_tensor_tensor(out=h1_lo[:, n, :], in0=h_out(n), scalar=0.0,
                                                   in1=h1_hi[:, n, :].bitcast(fp32), op0=ALU.max,
                                                   op1=ALU.subtract).then_inc(s_h1lo, 1)

            def split_z(i):
                dve.wait_ge(s_zhi, i * (1 + NZ) + 1)
                nc.vector.tensor_sub(z_lo[:, 0, :].rearrange("p (q j) -> p q j", q=Q),
                                     dense_t[:, :, bass.ds(i * SJ, SJ)],
                                     z_hi[:, 0, :].bitcast(fp32).rearrange("p (q j) -> p q j", q=Q)
                                     ).then_inc(s_zlo, 1)
                for c in range(NZ):
                    dve.wait_ge(s_zhi, i * (1 + NZ) + c + 2)
                    nc.vector.tensor_sub(z_lo[0:ZR[c], 1 + c, :], z[0:ZR[c], 1 + c, :],
                                         z_hi[0:ZR[c], 1 + c, :].bitcast(fp32)).then_inc(s_zlo, 1)

            def row_copies(i, t, last=False):
                copy_items("dve", dve, nc.vector.tensor_copy, i, "rows", t)
                if not last:
                    stage_ids(i, t)

            def step(i, ahead=NO, last=False):
                make_onehot(i, range(ahead, HS - NO), False)
                split_z(i - 1)
                row_copies(i, 0, last)
                make_onehot(i, range(HS - NO, HS), False)
                for t in range(TS):
                    put_dense(i, t, False)
                relu_one(i - 1, range(H1C))
                copy_chunks(i, 0)
                row_copies(i, 1, last)
                if not last:
                    make_onehot(i + 1, range(NO), False)
                copy_chunks(i, 1)

            def split_low(x):
                dve.wait_ge(s_hi, x + 1)
                nc.vector.tensor_sub(tab_lo[0:PK, x].rearrange("p k d -> p (k d)"),
                                     staged[0:PK, x % NSTAGE, :],
                                     tab_hi[0:PK, x].rearrange("p k d -> p (k d)").bitcast(fp32)).then_inc(s_lo, 1)

            split_low(0)
            make_onehot(0, range(NO), True)
            for x in range(1, NX):
                split_low(x)
                make_onehot(0, range(NO * x, NO * (x + 1)), True)
            dve.wait_ge(s_hi, NX + 1)
            nc.vector.tensor_sub(w2_lo[:].rearrange("p c n -> p (c n)"), staged[:, NX % NSTAGE, :],
                                 w2_hi[:].rearrange("p c n -> p (c n)").bitcast(fp32)).then_inc(s_lo, 1)
            dve.wait_ge(s_w1, 16 * 2)
            nc.vector.tensor_add(w1raw[:, 0, :], w1raw[:, 0, :], w1second).then_inc(s_w1sum, 1)
            dve.wait_ge(s_dcopy, NT // 4)
            for t in range(TS):
                put_dense(0, t, True)
            row_copies(0, 0)
            make_onehot(1, range(NO), False)
            copy_chunks(0, 0)
            make_onehot(1, range(NO, 2 * NO), False)
            row_copies(0, 1)
            make_onehot(1, range(2 * NO, 3 * NO), False)
            dve.wait_ge(s_w1hi, 1)
            nc.vector.tensor_sub(w1_lo[:], w1raw, w1_hi[:].bitcast(fp32)).then_inc(s_w1lo, 1)
            copy_chunks(0, 1)
            step(1, ahead=3 * NO)
            with dve.Fori(2, NS - 1) as i:
                step(i)
            step(NS - 1, last=True)
            split_z(NS - 1)
            relu_one(NS - 1, range(H1C))


_TABLES = [f"tbl_{f}" for f in range(F)]
_INS = ["r_dense_features", *_TABLES, "W_top2", "b_top2", "W_top3"]
_COLUMNS = ["b_top2", "W_top3"]


def kernel(**inputs):
    import numpy as np
    import concourse.bacc as bacc
    from concourse.bass_utils import run_bass_kernel_spmd as run

    nc = bacc.Bacc("TRN2", target_bir_lowering=False, num_devices=1)
    arrays, a = {}, {}

    def give(name, x):
        x = np.ascontiguousarray(x)
        arrays[f"in_{name}"] = x
        a[name] = nc.dram_tensor(f"in_{name}", x.shape, mybir.dt.from_np(x.dtype), kind="ExternalInput").ap()

    for name in _INS:
        x = np.asarray(inputs[name])
        if name in _COLUMNS:
            x = x.reshape(-1, P).T
        give(name, x)
    w = np.asarray(inputs["W_top1"])
    zeros = np.zeros((1, N1), w.dtype)
    chunks = [w[0:D]] + [np.concatenate([zeros if r is None else w[r:r + 1] for r in rows]) for rows in pair_rows()]
    chunks[NZ][ZR[-1]] = np.asarray(inputs["b_top1"])
    give("W_top1", np.stack(chunks + [w[D + NPAIR:]], axis=1))
    ids = np.asarray(inputs["ids"])
    give("ids", ids.reshape(Q, NT, JJ, F).transpose(0, 2, 1, 3).reshape(P, NT * F))
    ids = ids[:, list(LOOKED)].reshape(Q, NS, SJ, NX)
    give("ids_steps", ids.transpose(1, 3, 0, 2).reshape(NS, NX * SB))
    out = nc.dram_tensor("out_y", (B, 1), fp32, kind="ExternalOutput").ap()
    build(nc, a["r_dense_features"], a["ids"], a["ids_steps"], [a[t] for t in _TABLES], a["W_top1"],
          a["W_top2"], a["b_top2"], a["W_top3"], out)
    r = run(nc, [arrays], core_ids=[0])
    return r.results[0]["out_y"]
```
